# Optimizing a Trainium2 kernel written in Bass

```python
import numpy as np
import jax
import jax.numpy as jnp

def _softmax(x, axis=-1):
    return jax.nn.softmax(x, axis=axis)

def _gelu(x):
    return jax.nn.gelu(x, approximate=True)

def _silu(x):
    return jax.nn.silu(x)

def _sigmoid(x):
    return jax.nn.sigmoid(x)

def _layernorm(x, axis=-1, eps=1e-05):
    m = jnp.mean(x, axis=axis, keepdims=True)
    v = jnp.var(x, axis=axis, keepdims=True)
    return (x - m) / jnp.sqrt(v + eps)

def _scatter_add(tgt, idx, src, axis=0):
    return tgt.at[idx].add(src)

def _segment_sum(src, seg, n):
    return jax.ops.segment_sum(src, seg, n)
kernel_name = 'mk_rec_standalone_d1_rec_r8_cb001e'

def setup_inputs(seed: int=0):
    np.random.seed(seed)
    _w = jnp.asarray

    def _rec_inputs():
        import jax
        import jax.numpy as jnp
        _rk = jax.random.key(seed)
        r_inputs = -0.000849101 + 1.0004 * jax.random.normal(jax.random.fold_in(_rk, 1), (512, 39, 16), jnp.float32)
        return r_inputs
    r_inputs = _rec_inputs()

    def _L0_rec_setup():
        import jax, jax.numpy as jnp
        import numpy as np
        B, F0, D = (256, 39, 16)
        LAYER_SIZES = [128, 128, 128]
        key = jax.random.key(seed)
        ks = jax.random.split(key, 1 + 2 * len(LAYER_SIZES))
        inputs = jax.random.normal(ks[0], (B, F0, D), dtype=jnp.float32)
        out = {'inputs': inputs}
        field_nums = [F0]
        for i, size in enumerate(LAYER_SIZES):
            fk = field_nums[-1]
            fan_in = F0 * fk
            scale = np.sqrt(2.0 / (fan_in + size)).astype(np.float32)
            out[f'w{i}'] = jax.random.normal(ks[1 + 2 * i], (F0, fk, size), dtype=jnp.float32) * scale
            out[f'b{i}'] = jnp.zeros((size,), dtype=jnp.float32)
            field_nums.append(size // 2)
        return out
    _L0_rec_all = _L0_rec_setup()
    _L0_rec_in = {k: v for k, v in _L0_rec_all.items() if k in ('w0', 'w1', 'w2', 'b0', 'b1', 'b2')}
    del _L0_rec_all
    return {'r_inputs': r_inputs, 'L0_rec_w0': _L0_rec_in['w0'], 'L0_rec_w1': _L0_rec_in['w1'], 'L0_rec_w2': _L0_rec_in['w2'], 'L0_rec_b0': _L0_rec_in['b0'], 'L0_rec_b1': _L0_rec_in['b1'], 'L0_rec_b2': _L0_rec_in['b2']}

def reference(r_inputs, L0_rec_w0, L0_rec_w1, L0_rec_w2, L0_rec_b0, L0_rec_b1, L0_rec_b2):
    import jax
    import jax.numpy as jnp

    def _L0_rec_ref(inputs, w0, w1, w2, b0, b1, b2):
        import jax, jax.numpy as jnp
        import numpy as np
        B, F0, D = (256, 39, 16)
        LAYER_SIZES = [128, 128, 128]
        x0 = inputs
        xk = inputs
        params = [(w0, b0), (w1, b1), (w2, b2)]
        n_layers = len(params)
        direct = []
        for idx, (W, b) in enumerate(params):
            z = jnp.einsum('bhd,bkd,hks->bsd', x0, xk, W) + b[None, :, None]
            z = jax.nn.relu(z)
            if idx != n_layers - 1:
                half = z.shape[1] // 2
                xk = z[:, :half, :]
                direct.append(z[:, half:, :])
            else:
                direct.append(z)
        logit = jnp.sum(jnp.concatenate(direct, axis=1), axis=-1)
        return logit
    y = _L0_rec_ref(r_inputs, L0_rec_w0, L0_rec_w1, L0_rec_w2, L0_rec_b0, L0_rec_b1, L0_rec_b2)
    return y

_drawn_inputs = setup_inputs


def setup_inputs(seed=0):
    import zlib

    import numpy as np

    out = dict(_drawn_inputs(seed))
    spreads = {'L0_rec_b0': (0.0, 0.1), 'L0_rec_b1': (0.0, 0.1), 'L0_rec_b2': (0.0, 0.1)}
    factors = {}
    for name, (base, spread) in spreads.items():
        noise = np.random.default_rng([zlib.crc32(name.encode()), seed]).standard_normal(out[name].shape)
        drawn = base * np.exp(spread * noise) if base else spread * noise
        out[name] = jnp.asarray(drawn.astype(out[name].dtype))
    for name, factor in factors.items():
        out[name] = (out[name] * factor).astype(out[name].dtype)
    return out
```

```python
import concourse.bass as bass
from concourse import mybir
from contextlib import ExitStack

FIELDS = 39
DIM = 16
BATCH = 512
OUT = 128
HALF = OUT // 2
COLS = 512
EXAMPLES = COLS // DIM
CHUNKS = BATCH * DIM // COLS
SHIFTS = FIELDS // 2 + 1
GROUP = 3
ROWS0 = GROUP * FIELDS
TILES0 = -(-SHIFTS // GROUP)
LAST0 = (SHIFTS - GROUP * (TILES0 - 1)) * FIELDS
TILES = (FIELDS + 1) // 2
RING = 4


def cin_kernel(nc, x0, w0a, w0b, w1, w2, b0, b1, b2, out):
    fp32 = mybir.dt.float32
    ALU = mybir.AluOpType
    ACT = mybir.ActivationFunctionType
    AX = mybir.AxisListType

    ctx = ExitStack()
    with ctx:
        def sb(name, shape):
            return ctx.enter_context(nc.sbuf_tensor(name, shape, fp32))

        def pb(name, shape):
            return ctx.enter_context(nc.psum_tensor(name, shape, fp32))

        def sem(name):
            return ctx.enter_context(nc.semaphore(name))

        w0_sb = sb("w0_sb", [128, TILES0, OUT])
        w0t_sb = sb("w0t_sb", [128, TILES0, OUT])
        w1_sb = sb("w1_sb", [128, TILES, OUT])
        w2_sb = sb("w2_sb", [128, TILES, OUT])
        bias = sb("bias", [128, 3])
        field_copies = sb("field_copies", [128, 2, COLS])
        field_shifts = sb("field_shifts", [128, 2, TILES0, COLS])
        field_spread = sb("field_spread", [128, 2, TILES, COLS])
        products = sb("products", [128, RING, 2, COLS])
        maps1 = sb("maps1", [128, COLS])
        maps2 = sb("maps2", [128, COLS])
        direct = sb("direct", [128, 2, COLS])
        last = sb("last", [128, COLS])
        sums = sb("sums", [128, 2, BATCH])

        z0 = pb("z0", [128, COLS])
        z1 = pb("z1", [128, COLS])
        z2 = pb("z2", [128, COLS])

        w0_loaded = sem("w0_loaded")
        w1_loaded = sem("w1_loaded")
        w2_loaded = sem("w2_loaded")
        bias_loaded = sem("bias_loaded")
        fields_loaded = [sem("fields_loaded0"), sem("fields_loaded1")]
        spread_loaded = [[sem(f"spread_loaded{p}{q}") for q in range(2)] for p in range(2)]
        w0_summed = sem("w0_summed")
        products_ready = sem("products_ready")
        products_used = sem("products_used")
        z0_evacuated = sem("z0_evacuated")
        z1_evacuated = sem("z1_evacuated")
        z2_evacuated = sem("z2_evacuated")
        direct_summed = sem("direct_summed")
        last_summed = sem("last_summed")
        stored = sem("stored")

        PAIRS0 = (TILES0 + 1) // 2
        PAIRS = TILES // 2
        PER_ROUND = PAIRS0 + 2 * PAIRS
        assert PAIRS0 % RING == 0 and PER_ROUND % RING == 0

        def at_layer1(c):
            return PAIRS0 + PER_ROUND * c

        def at_layer0(c):
            return at_layer1(c - 1) + PAIRS

        def at_layer2(c):
            return at_layer1(c) + PAIRS + PAIRS0

        SLOT1, SLOT0, SLOT2 = 0, PAIRS % RING, (PAIRS + PAIRS0) % RING

        def chunk(i, d):
            return 2 * i + d, d % 2, i + d // 2 + 1

        block = ctx.enter_context(nc.Block())

        @block.sync
        def _(sp):
            def load_fields(c, par):
                for g in range(GROUP):
                    sp.dma_start(field_copies[g * FIELDS:(g + 1) * FIELDS, par, :],
                                 x0[c, 0:FIELDS, :]).then_inc(fields_loaded[par], 16)
                for g in range(GROUP):
                    n = TILES0 if g < SHIFTS - GROUP * (TILES0 - 1) else TILES0 - 1
                    base = x0[c, g:g + FIELDS, :]
                    src = bass.AP(tensor=base.tensor, offset=base.offset,
                                  ap=[[COLS, FIELDS], [GROUP * COLS, n], [1, COLS]])
                    sp.dma_start(field_shifts[g * FIELDS:(g + 1) * FIELDS, par, 0:n, :],
                                 src).then_inc(fields_loaded[par], 16)

            def load_spread(c, par, q):
                lo, hi = ((0, TILES // 2), (TILES // 2, TILES))[q]
                for half in range(2):
                    n = hi - lo
                    base = x0[c, 2 * lo + half:2 * lo + half + 1, :]
                    src = bass.AP(tensor=base.tensor, offset=base.offset,
                                  ap=[[0, HALF], [2 * COLS, n], [1, COLS]])
                    sp.dma_start(field_spread[half * HALF:(half + 1) * HALF, par, lo:lo + n, :],
                                 src).then_inc(spread_loaded[par][q], 16)

            load_fields(0, 0)
            load_spread(0, 0, 0)
            load_spread(0, 0, 1)
            load_fields(1, 1)
            load_spread(1, 1, 0)
            load_spread(1, 1, 1)
            sp.wait_ge(products_ready, PAIRS0)
            load_fields(2, 0)

            def refill(c, par, more_fields=True):
                if more_fields:
                    sp.wait_ge(products_ready, at_layer0(c + 1) + PAIRS0)
                    load_fields(c + 3, 1 - par)
                sp.wait_ge(products_ready, at_layer2(c) + PAIRS // 2)
                load_spread(c + 2, par, 0)
                sp.wait_ge(products_ready, at_layer2(c) + PAIRS)
                load_spread(c + 2, par, 1)

            with sp.Fori(0, CHUNKS // 2 - 2) as i:
                refill(2 * i, 0)
                refill(2 * i + 1, 1)
            refill(CHUNKS - 4, 0)
            refill(CHUNKS - 3, 1, more_fields=False)

            sp.wait_ge(direct_summed, CHUNKS)
            sp.dma_start(out[0:OUT, :], sums[:, 0, :]).then_inc(stored, 16)
            sp.wait_ge(last_summed, CHUNKS)
            sp.dma_start(out[OUT:2 * OUT, :], sums[:, 1, :]).then_inc(stored, 16)
            sp.wait_ge(stored, 32)

        @block.vector
        def _(dve):
            def multiply0(c, par, use, base, slot, first=False):
                dve.wait_ge(fields_loaded[par], use * 2 * GROUP * 16)
                for k in range(PAIRS0):
                    if not first:
                        dve.wait_ge(products_used, base + k - RING + 1)
                    t, n = 2 * k, min(2, TILES0 - 2 * k)
                    rows = ROWS0 if t + n < TILES0 else LAST0
                    copies = field_copies[0:rows, par, :].unsqueeze(1).to_broadcast([rows, n, COLS])
                    nc.vector.tensor_tensor(products[0:rows, (slot + k) % RING, 0:n, :],
                                            field_shifts[0:rows, par, t:t + n, :], copies,
                                            ALU.mult).then_inc(products_ready, 1)

            def multiply(par, use, maps, base, slot, ks, wait_spread):
                for k in ks:
                    if wait_spread and k in (0, PAIRS // 2):
                        dve.wait_ge(spread_loaded[par][k // (PAIRS // 2)], use * 32)
                    dve.wait_ge(products_used, base + k - RING + 1)
                    s = (slot + k) % RING
                    nc.vector.tensor_tensor(products[:, s, :, :], field_spread[:, par, 2 * k:2 * k + 2, :],
                                            maps[:, :].unsqueeze(1).to_broadcast([128, 2, COLS]),
                                            ALU.mult).then_inc(products_ready, 1)

            def sum_direct(c, par):
                dve.wait_ge(z0_evacuated, 3 * c + 3)
                dve.wait_ge(z1_evacuated, 3 * c + 3)
                nc.vector.tensor_reduce(sums[:, 0, bass.ds(c * EXAMPLES, EXAMPLES)],
                                        direct[:, par, :].rearrange("p (b d) -> p b d", d=DIM),
                                        AX.X, ALU.add).then_inc(direct_summed, 1)

            def sum_last(c):
                dve.wait_ge(z2_evacuated, c + 1)
                nc.vector.tensor_reduce(sums[:, 1, bass.ds(c * EXAMPLES, EXAMPLES)],
                                        last[:, :].rearrange("p (b d) -> p b d", d=DIM),
                                        AX.X, ALU.add).then_inc(last_summed, 1)

            def round(i, d, first=False, more=True):
                c, par, use = chunk(i, d)
                early, late = range(0, PAIRS // 2), range(PAIRS // 2, PAIRS)
                dve.wait_ge(z0_evacuated, 3 * c + 2)
                multiply(par, use, maps1, at_layer1(c), SLOT1, early, True)
                if not first:
                    sum_last(c - 1)
                multiply(par, use, maps1, at_layer1(c), SLOT1, late, True)
                if more:
                    multiply0(*chunk(i, d + 1), at_layer0(c + 1), SLOT0)
                at2 = at_layer2(c) if more else at_layer0(c + 1)
                slot2 = SLOT2 if more else SLOT0
                dve.wait_ge(z1_evacuated, 3 * c + 2)
                multiply(par, use, maps2, at2, slot2, early, False)
                sum_direct(c, par)
                multiply(par, use, maps2, at2, slot2, late, False)

            dve.wait_ge(w0_loaded, 32)
            nc.vector.tensor_tensor(w0_sb[0:ROWS0, :, :], w0_sb[0:ROWS0, :, :], w0t_sb[0:ROWS0, :, :],
                                    ALU.add).then_inc(w0_summed, 1)
            multiply0(0, 0, 1, 0, 0, first=True)
            round(0, 0, first=True)
            with dve.Fori(0, CHUNKS // 2 - 1) as i:
                round(i, 1)
                round(i, 2)
            round(CHUNKS // 2 - 1, 1, more=False)
            sum_last(CHUNKS - 1)

        @block.tensor
        def _(pe):
            def contract(z, weights, tiles, short, base, slot):
                for t in range(tiles):
                    k, j = t // 2, t % 2
                    if j == 0:
                        pe.wait_ge(products_ready, base + k + 1)
                    rows = short if t == tiles - 1 else ROWS0 if tiles == TILES0 else 128
                    mm = nc.tensor.matmul(z[:, :], weights[0:rows, t, :], products[0:rows, (slot + k) % RING, j, :],
                                          start=(t == 0), stop=(t == tiles - 1))
                    if j == 1 or t == tiles - 1:
                        mm.then_inc(products_used, 1)

            def round(i, d, first=False, more=True):
                c, _, _ = chunk(i, d)
                if not first:
                    pe.wait_ge(z1_evacuated, 3 * c)
                contract(z1, w1_sb, TILES, HALF, at_layer1(c), SLOT1)
                if more:
                    pe.wait_ge(z0_evacuated, 3 * c + 3)
                    contract(z0, w0_sb, TILES0, LAST0, at_layer0(c + 1), SLOT0)
                if first:
                    pe.wait_ge(w2_loaded, 32)
                else:
                    pe.wait_ge(z2_evacuated, c)
                contract(z2, w2_sb, TILES, HALF, at_layer2(c) if more else at_layer0(c + 1),
                         SLOT2 if more else SLOT0)

            pe.wait_ge(w0_summed, 1)
            contract(z0, w0_sb, TILES0, LAST0, 0, 0)
            pe.wait_ge(w1_loaded, 32)
            round(0, 0, first=True)
            with pe.Fori(0, CHUNKS // 2 - 1) as i:
                round(i, 1)
                round(i, 2)
            round(CHUNKS // 2 - 1, 1, more=False)

        @block.scalar
        def _(act):
            for half_w, w_sb in ((w0a, w0_sb), (w0b, w0t_sb)):
                act.dma_start(w_sb[0:ROWS0, :, :], half_w).then_inc(w0_loaded, 16)
            for n, b in enumerate((b0, b1, b2)):
                act.dma_start(bias[:, n:n + 1], b).then_inc(bias_loaded, 16)
            for w, w_sb, w_loaded in ((w1, w1_sb, w1_loaded), (w2, w2_sb, w2_loaded)):
                whole = (TILES - 1) * 128
                act.dma_start(w_sb[:, 0:TILES - 1, :],
                              w[0:whole, :].rearrange("(t p) s -> p t s", p=128)).then_inc(w_loaded, 16)
                act.dma_start(w_sb[0:HALF, TILES - 1, :], w[whole:whole + HALF, :]).then_inc(w_loaded, 16)

            def spread_maps(z, layer, maps, direct_out, evacuated):
                for half in range(2):
                    nc.scalar.activation(maps[half * HALF:(half + 1) * HALF, :], z[0:HALF, :], ACT.Relu,
                                         bias=bias[0:HALF, layer:layer + 1]).then_inc(evacuated, 1)
                nc.scalar.activation(direct_out, z[HALF:OUT, :], ACT.Relu,
                                     bias=bias[HALF:OUT, layer:layer + 1]).then_inc(evacuated, 1)

            def round(i, d, first=False, more=True):
                c, par, _ = chunk(i, d)
                act.wait_ge(products_used, at_layer1(c) + PAIRS)
                spread_maps(z1, 1, maps2, direct[HALF:OUT, par, :], z1_evacuated)
                if more:
                    act.wait_ge(products_used, at_layer0(c + 1) + PAIRS0)
                    if not first:
                        act.wait_ge(direct_summed, c)
                    spread_maps(z0, 0, maps1, direct[0:HALF, 1 - par, :], z0_evacuated)
                at2 = at_layer2(c) if more else at_layer0(c + 1)
                act.wait_ge(products_used, at2 + PAIRS)
                if not first:
                    act.wait_ge(last_summed, c)
                nc.scalar.activation(last[:, :], z2[:, :], ACT.Relu,
                                     bias=bias[:, 2:3]).then_inc(z2_evacuated, 1)

            act.wait_ge(bias_loaded, 48)
            act.wait_ge(products_used, PAIRS0)
            spread_maps(z0, 0, maps1, direct[0:HALF, 0, :], z0_evacuated)
            round(0, 0, first=True)
            with act.Fori(0, CHUNKS // 2 - 1) as i:
                round(i, 1)
                round(i, 2)
            round(CHUNKS // 2 - 1, 1, more=False)


def kernel(r_inputs, L0_rec_w0, L0_rec_w1, L0_rec_w2, L0_rec_b0, L0_rec_b1, L0_rec_b2):
    import numpy as np
    import concourse.bacc as bacc
    from concourse import mybir as mb
    from concourse.bass_utils import run_bass_kernel_spmd

    x = np.asarray(r_inputs).reshape(CHUNKS, EXAMPLES, FIELDS, DIM).transpose(0, 2, 1, 3)
    x = x.reshape(CHUNKS, FIELDS, COLS)
    w0 = np.asarray(L0_rec_w0)
    w0a = np.zeros((GROUP, FIELDS, TILES0, OUT), w0.dtype)
    w0b = np.zeros((GROUP, FIELDS, TILES0, OUT), w0.dtype)
    i = np.arange(FIELDS)
    for shift in range(SHIFTS):
        t, g = divmod(shift, GROUP)
        j = (i + shift) % FIELDS
        w0a[g, :, t] = w0[i, j]
        if shift:
            w0b[g, :, t] = w0[j, i]
    arrays = {
        "x0": np.concatenate([x, x], axis=1),
        "w0a": w0a.reshape(ROWS0, TILES0, OUT),
        "w0b": w0b.reshape(ROWS0, TILES0, OUT),
        "w1": np.asarray(L0_rec_w1).reshape(FIELDS * HALF, OUT),
        "w2": np.asarray(L0_rec_w2).reshape(FIELDS * HALF, OUT),
        "b0": np.asarray(L0_rec_b0).reshape(OUT, 1),
        "b1": np.asarray(L0_rec_b1).reshape(OUT, 1),
        "b2": np.asarray(L0_rec_b2).reshape(OUT, 1),
    }
    nc = bacc.Bacc("TRN2", target_bir_lowering=False, num_devices=1)
    args = []
    for name, a in arrays.items():
        arrays[name] = np.ascontiguousarray(a)
        args.append(nc.dram_tensor(name, a.shape, mb.dt.from_np(a.dtype), kind="ExternalInput").ap())
    args.append(nc.dram_tensor("out", (2 * OUT, BATCH), mb.dt.float32, kind="ExternalOutput").ap())
    cin_kernel(nc, *args)
    r = run_bass_kernel_spmd(nc, [arrays], core_ids=[0])
    return np.ascontiguousarray(r.results[0]["out"].T)
```

```python
import concourse.bass as bass
from concourse import mybir
from contextlib import ExitStack

FIELDS = 39
DIM = 16
BATCH = 512
OUT = 128
HALF = OUT // 2
COLS = 512
EXAMPLES = COLS // DIM
CHUNKS = BATCH * DIM // COLS
SHIFTS = FIELDS // 2 + 1
GROUP = 3
ROWS0 = GROUP * FIELDS
TILES0 = -(-SHIFTS // GROUP)
LAST0 = (SHIFTS - GROUP * (TILES0 - 1)) * FIELDS
TILES = (FIELDS + 1) // 2

E, S = "E", "S"
KINDS = ("SSEE", "ESESSSEESE", "ESSEESSESE")
COUPLES = tuple(len(k) for k in KINDS)
SPLIT_TILES = tuple(2 * k.count(S) for k in KINDS)
EXACT_TILES = (TILES0 - SPLIT_TILES[0], TILES - SPLIT_TILES[1], TILES - SPLIT_TILES[2])
LO_LAG = 2

EXACT_RING = 4
RAW_RING = 3
HI_RING = 3
LO_RING = 4


def tiles_of(layer, kind):
    tiles = (TILES0, TILES, TILES)[layer]
    return [t for t in range(tiles) if KINDS[layer][t // 2] == kind]


STEPS = (1, 0, 2)
PER_ROUND = {k: sum(kinds.count(k) for kinds in KINDS) for k in (E, S)}
for _ring, _kind in ((EXACT_RING, E), (RAW_RING, S), (HI_RING, S), (LO_RING, S)):
    assert 2 * PER_ROUND[_kind] % _ring == 0


def place(kind, i, d, layer, more=True):
    before = {1: 0, 0: KINDS[1].count(kind), 2: KINDS[1].count(kind) + more * KINDS[0].count(kind)}[layer]
    first = KINDS[0].count(kind) + PER_ROUND[kind] * d + before
    return first + 2 * PER_ROUND[kind] * i, first


def cin_kernel(nc, x0, w0e, w0s, w1e, w1s, w2e, w2s, b0, b1, b2, out):
    fp32 = mybir.dt.float32
    fp32r = mybir.dt.float32r
    ALU = mybir.AluOpType
    ACT = mybir.ActivationFunctionType
    AX = mybir.AxisListType

    ctx = ExitStack()
    with ctx:
        def sb(name, shape, dt=fp32):
            return ctx.enter_context(nc.sbuf_tensor(name, shape, dt))

        def pb(name, shape):
            return ctx.enter_context(nc.psum_tensor(name, shape, fp32))

        def sem(name):
            return ctx.enter_context(nc.semaphore(name))

        w_exact = [sb(f"w{n}_exact", [128, EXACT_TILES[n], OUT]) for n in range(3)]
        w_hi = [sb(f"w{n}_hi", [128, SPLIT_TILES[n], OUT], fp32r) for n in range(3)]
        w_lo = [sb(f"w{n}_lo", [128, SPLIT_TILES[n], OUT], fp32r) for n in range(3)]
        bias = sb("bias", [128, 3])
        field_copies = sb("field_copies", [128, COLS])
        field_shifts = sb("field_shifts", [128, TILES0, COLS])
        field_spread = sb("field_spread", [128, 2, TILES, COLS])
        exact = sb("exact", [128, EXACT_RING, 2, COLS])
        raw = sb("raw", [128, RAW_RING, 2, COLS])
        hi = sb("hi", [128, HI_RING, 2, COLS], fp32r)
        lo = sb("lo", [128, LO_RING, 2, COLS], fp32r)
        direct = sb("direct", [128, COLS])
        sums = sb("sums", [128, 2, BATCH])

        staging = field_spread[:, 1, :, :].rearrange("p t c -> p (t c)")
        at = 0
        w_staged = []
        for n in range(3):
            size = SPLIT_TILES[n] * OUT
            w_staged.append(staging[:, at:at + size].rearrange("p (t s) -> p t s", s=OUT))
            at += size
        w0s_t = staging[:, at:at + SPLIT_TILES[0] * OUT].rearrange("p (t s) -> p t s", s=OUT)
        at += SPLIT_TILES[0] * OUT
        w0e_t = staging[:, at:at + EXACT_TILES[0] * OUT].rearrange("p (t s) -> p t s", s=OUT)

        z = [pb(f"z{n}", [128, COLS]) for n in range(3)]
        maps1 = pb("maps1", [128, COLS])
        maps2 = pb("maps2", [128, COLS])
        copies = pb("copies", [128, COLS])

        w0_loaded = sem("w0_loaded")
        w_staged_loaded = [None, sem("w1_staged_loaded"), sem("w2_staged_loaded")]
        w_exact_loaded = [None, sem("w1_exact_loaded"), sem("w2_exact_loaded")]
        w0_summed = sem("w0_summed")
        weights_hi = sem("weights_hi")
        weights_lo = sem("weights_lo")
        bias_loaded = sem("bias_loaded")
        fields_loaded = sem("fields_loaded")
        spread_loaded = [[sem(f"spread_loaded{p}{q}") for q in range(2)] for p in range(2)]
        copies_ready = sem("copies_ready")
        exact_ready = sem("exact_ready")
        exact_used = sem("exact_used")
        raw_ready = sem("raw_ready")
        hi_ready = sem("hi_ready")
        hi_used = sem("hi_used")
        lo_ready = sem("lo_ready")
        lo_used = sem("lo_used")
        z0_evacuated = sem("z0_evacuated")
        z1_evacuated = sem("z1_evacuated")
        z2_evacuated = sem("z2_evacuated")
        direct_summed = sem("direct_summed")
        last_summed = sem("last_summed")
        stored = sem("stored")

        def loads(i, d):
            return i + d // 2 + 1

        EARLY = COUPLES[1] // 2

        block = ctx.enter_context(nc.Block())

        @block.sync
        def _(sp):
            def load_fields(c):
                for g in range(GROUP):
                    sp.dma_start(field_copies[g * FIELDS:(g + 1) * FIELDS, :],
                                 x0[c, 0:FIELDS, :]).then_inc(fields_loaded, 16)
                for g in range(GROUP):
                    n = TILES0 if g < SHIFTS - GROUP * (TILES0 - 1) else TILES0 - 1
                    base = x0[c, g:g + FIELDS, :]
                    src = bass.AP(tensor=base.tensor, offset=base.offset,
                                  ap=[[COLS, FIELDS], [GROUP * COLS, n], [1, COLS]])
                    sp.dma_start(field_shifts[g * FIELDS:(g + 1) * FIELDS, 0:n, :],
                                 src).then_inc(fields_loaded, 16)

            def load_spread(c, par, q):
                start, end = ((0, 2 * EARLY), (2 * EARLY, TILES))[q]
                for half in range(2):
                    base = x0[c, 2 * start + half:2 * start + half + 1, :]
                    src = bass.AP(tensor=base.tensor, offset=base.offset,
                                  ap=[[0, HALF], [2 * COLS, end - start], [1, COLS]])
                    sp.dma_start(field_spread[half * HALF:(half + 1) * HALF, par, start:end, :],
                                 src).then_inc(spread_loaded[par][q], 16)

            def wait_multiplied(i, d, layer, couples):
                kind = KINDS[layer][couples - 1]
                sp.wait_ge(exact_ready if kind == E else raw_ready,
                           place(kind, i, d, layer)[0] + KINDS[layer][:couples].count(kind))

            load_fields(0)
            load_spread(0, 0, 0)
            load_spread(0, 0, 1)
            for kind, ready in ((E, exact_ready), (S, raw_ready)):
                sp.wait_ge(ready, KINDS[0].count(kind))
            load_fields(1)
            sp.wait_ge(weights_lo, 3)
            load_spread(1, 1, 0)
            load_spread(1, 1, 1)

            def refill(i, d, more_spread=True):
                c = 2 * i + d
                wait_multiplied(i, d, 0, COUPLES[0])
                load_fields(c + 2)
                if more_spread:
                    wait_multiplied(i, d, 2, EARLY)
                    load_spread(c + 2, d % 2, 0)
                    wait_multiplied(i, d, 2, COUPLES[2])
                    load_spread(c + 2, d % 2, 1)

            with sp.Fori(0, CHUNKS // 2 - 1) as i:
                refill(i, 0)
                refill(i, 1)

            sp.wait_ge(direct_summed, CHUNKS)
            sp.dma_start(out[0:OUT, :], sums[:, 0, :]).then_inc(stored, 16)
            sp.wait_ge(last_summed, CHUNKS)
            sp.dma_start(out[OUT:2 * OUT, :], sums[:, 1, :]).then_inc(stored, 16)
            sp.wait_ge(stored, 32)

        @block.vector
        def _(dve):
            def multiply(layer, by, spread, rows_of, counts, couples, started):
                n = {}
                for kind in (E, S):
                    count, slot = counts[kind]
                    skip = KINDS[layer][:couples[0]].count(kind)
                    n[kind] = [count + skip, slot + skip]
                for k in couples:
                    kind = KINDS[layer][k]
                    count, slot = n[kind]
                    tiles = min(2, (TILES0, TILES, TILES)[layer] - 2 * k)
                    rows = rows_of(k)
                    if kind == E:
                        if started or slot >= EXACT_RING:
                            dve.wait_ge(exact_used, count - EXACT_RING + 1)
                        ring, ready = exact[0:rows, slot % EXACT_RING, 0:tiles, :], exact_ready
                    else:
                        if started or slot >= RAW_RING:
                            dve.wait_ge(lo_ready, count - RAW_RING + 1)
                        ring, ready = raw[0:rows, slot % RAW_RING, 0:tiles, :], raw_ready
                    nc.vector.tensor_tensor(ring, spread[0:rows, 2 * k:2 * k + tiles, :],
                                            by[0:rows, :].unsqueeze(1).to_broadcast([rows, tiles, COLS]),
                                            ALU.mult).then_inc(ready, 1)
                    n[kind] = [count + 1, slot + 1]

            def multiply0(c, counts, started=True):
                dve.wait_ge(fields_loaded, (c + 1) * 2 * GROUP * 16)
                dve.wait_ge(copies_ready, c + 1)
                multiply(0, copies, field_shifts, lambda k: ROWS0 if k < COUPLES[0] - 1 else LAST0, counts,
                         range(COUPLES[0]), started)

            def multiply12(layer, i, d, couples, more=True, started=True):
                counts = {kind: place(kind, i, d, layer, more) for kind in (E, S)}
                multiply(layer, maps1 if layer == 1 else maps2, field_spread[:, d % 2, :, :],
                         lambda k: 128, counts, couples, started)

            def sum_direct(c):
                dve.wait_ge(z0_evacuated, 3 * c + 3)
                dve.wait_ge(z1_evacuated, 3 * c + 3)
                nc.vector.tensor_reduce(sums[:, 0, bass.ds(c * EXAMPLES, EXAMPLES)],
                                        direct[:, :].rearrange("p (b d) -> p b d", d=DIM),
                                        AX.X, ALU.add).then_inc(direct_summed, 1)

            def sum_last(c):
                dve.wait_ge(z2_evacuated, c + 1)
                nc.vector.tensor_reduce(sums[:, 1, bass.ds(c * EXAMPLES, EXAMPLES)],
                                        z[2][:, :].rearrange("p (b d) -> p b d", d=DIM),
                                        AX.X, ALU.add).then_inc(last_summed, 1)

            def round(i, d, first=False, more=True):
                c = 2 * i + d
                dve.wait_ge(z0_evacuated, 3 * c + 2)
                dve.wait_ge(spread_loaded[d % 2][0], loads(i, d) * 32)
                multiply12(1, i, d, range(0, EARLY), started=not first)
                dve.wait_ge(spread_loaded[d % 2][1], loads(i, d) * 32)
                multiply12(1, i, d, range(EARLY, 8), started=not first)
                if not first:
                    sum_last(c - 1)
                multiply12(1, i, d, range(8, COUPLES[1]), started=not first)
                if more:
                    multiply0(c + 1, {kind: place(kind, i, d, 0) for kind in (E, S)})
                dve.wait_ge(z1_evacuated, 3 * c + 2)
                multiply12(2, i, d, range(0, 6), more)
                sum_direct(c)
                multiply12(2, i, d, range(6, COUPLES[2]), more)

            def split_lo(n):
                rows = ROWS0 if n == 0 else 128
                dve.wait_ge(weights_hi, n + 1)
                nc.vector.tensor_tensor(w_lo[n][0:rows, :, :], w_staged[n][0:rows, :, :],
                                        w_hi[n][0:rows, :, :].bitcast(fp32), ALU.subtract).then_inc(weights_lo, 1)

            dve.wait_ge(w0_loaded, 64)
            nc.vector.tensor_tensor(w_staged[0][0:ROWS0, :, :], w_staged[0][0:ROWS0, :, :], w0s_t[0:ROWS0, :, :],
                                    ALU.add).then_inc(w0_summed, 1)
            nc.vector.tensor_tensor(w_exact[0][0:ROWS0, :, :], w_exact[0][0:ROWS0, :, :], w0e_t[0:ROWS0, :, :],
                                    ALU.add).then_inc(w0_summed, 1)
            split_lo(0)
            multiply0(0, {E: (0, 0), S: (0, 0)}, started=False)
            split_lo(1)
            split_lo(2)
            round(0, 0, first=True)
            with dve.Fori(0, CHUNKS // 2 - 1) as i:
                round(i, 1)
                round(i, 2)
            round(CHUNKS // 2 - 1, 1, more=False)
            sum_last(CHUNKS - 1)

        @block.gpsimd
        def _(pool):
            def split_lo(layer, count, slot, started=True):
                couples = [k for k in range(COUPLES[layer]) if KINDS[layer][k] == S]
                rows = ROWS0 if layer == 0 else 128
                for m in range(len(couples)):
                    pool.wait_ge(hi_ready, count + m + 1)
                    if started or slot + m >= LO_RING:
                        pool.wait_ge(lo_used, count + m - LO_RING + 1)
                    nc.gpsimd.tensor_tensor(lo[0:rows, (slot + m) % LO_RING, :, :],
                                            raw[0:rows, (slot + m) % RAW_RING, :, :],
                                            hi[0:rows, (slot + m) % HI_RING, :, :].bitcast(fp32),
                                            ALU.subtract).then_inc(lo_ready, 1)

            def round(i, d, first=False, more=True):
                split_lo(1, *place(S, i, d, 1), started=not first)
                if more:
                    split_lo(0, *place(S, i, d, 0))
                split_lo(2, *place(S, i, d, 2, more))

            split_lo(0, 0, 0, started=False)
            round(0, 0, first=True)
            with pool.Fori(0, CHUNKS // 2 - 1) as i:
                round(i, 1)
                round(i, 2)
            round(CHUNKS // 2 - 1, 1, more=False)

        @block.tensor
        def _(pe):
            def schedule(layer):
                todo, pending = [], []
                for k, kind in enumerate(KINDS[layer]):
                    todo.append(("exact" if kind == E else "hi", k))
                    if kind == S:
                        pending.append(k)
                    if pending and k - pending[0] >= LO_LAG:
                        todo.append(("lo", pending.pop(0)))
                tail = todo.pop() if todo[-1][0] == "exact" else None
                if tail is None:
                    tail = todo.pop(next(n for n in range(len(todo) - 1, -1, -1) if todo[n][0] == "exact"))
                return todo + [("lo", k) for k in pending] + [tail]

            def contract(layer, exact_at, split_at):
                tiles = (TILES0, TILES, TILES)[layer]
                order = schedule(layer)
                for step, (what, k) in enumerate(order):
                    kind = E if what == "exact" else S
                    count, slot = exact_at if kind == E else split_at
                    m = KINDS[layer][:k].count(kind)
                    ready = {"exact": exact_ready, "hi": hi_ready, "lo": lo_ready}[what]
                    pe.wait_ge(ready, count + m + 1)
                    n = min(2, tiles - 2 * k)
                    for j in range(n):
                        t = 2 * m + j
                        rows = ROWS0 if layer == 0 else 128
                        if 2 * k + j == tiles - 1:
                            rows = LAST0 if layer == 0 else HALF
                        if what == "exact":
                            passes = [(w_exact[layer], exact[0:rows, (slot + m) % EXACT_RING, j, :])]
                        elif what == "hi":
                            part = hi[0:rows, (slot + m) % HI_RING, j, :]
                            passes = [(w_hi[layer], part), (w_lo[layer], part)]
                        else:
                            passes = [(w_hi[layer], lo[0:rows, (slot + m) % LO_RING, j, :])]
                        for p, (w, part) in enumerate(passes):
                            mm = nc.tensor.matmul(z[layer][:, :], w[0:rows, t, :], part,
                                                  start=(step == 0 and j == 0 and p == 0),
                                                  stop=(step == len(order) - 1 and j == n - 1))
                    mm.then_inc({"exact": exact_used, "hi": hi_used, "lo": lo_used}[what], 1)

            def round(i, d, first=False, more=True):
                c = 2 * i + d
                if not first:
                    pe.wait_ge(z1_evacuated, 3 * c)
                contract(1, place(E, i, d, 1), place(S, i, d, 1))
                if more:
                    pe.wait_ge(z0_evacuated, 3 * c + 3)
                    contract(0, place(E, i, d, 0), place(S, i, d, 0))
                if first:
                    pe.wait_ge(w_exact_loaded[2], 16)
                    pe.wait_ge(weights_lo, 3)
                else:
                    pe.wait_ge(last_summed, c)
                contract(2, place(E, i, d, 2, more), place(S, i, d, 2, more))

            pe.wait_ge(w0_summed, 2)
            pe.wait_ge(weights_lo, 1)
            contract(0, (0, 0), (0, 0))
            pe.wait_ge(w_exact_loaded[1], 16)
            pe.wait_ge(weights_lo, 2)
            round(0, 0, first=True)
            with pe.Fori(0, CHUNKS // 2 - 1) as i:
                round(i, 1)
                round(i, 2)
            round(CHUNKS // 2 - 1, 1, more=False)

        @block.scalar
        def _(act):
            def split_hi(layer, counts, ms, started=True):
                count, slot = counts
                rows = ROWS0 if layer == 0 else 128
                for m in ms:
                    act.wait_ge(raw_ready, count + m + 1)
                    if started or slot + m >= HI_RING:
                        act.wait_ge(hi_used, count + m - HI_RING + 1)
                        act.wait_ge(lo_ready, count + m - HI_RING + 1)
                    nc.scalar.activation(hi[0:rows, (slot + m) % HI_RING, :, :],
                                         raw[0:rows, (slot + m) % RAW_RING, :, :],
                                         ACT.Copy).then_inc(hi_ready, 1)

            def weights_split_hi(n):
                rows = ROWS0 if n == 0 else 128
                nc.scalar.activation(w_hi[n][0:rows, :, :], w_staged[n][0:rows, :, :],
                                     ACT.Copy).then_inc(weights_hi, 1)

            def copy_fields(c):
                act.wait_ge(fields_loaded, (c + 1) * 2 * GROUP * 16)
                nc.scalar.activation(copies[0:ROWS0, :], field_copies[0:ROWS0, :], ACT.Copy).then_inc(copies_ready, 1)

            def spread_maps(n, maps, direct_out, evacuated):
                for half in range(2):
                    nc.scalar.activation(maps[half * HALF:(half + 1) * HALF, :], z[n][0:HALF, :], ACT.Relu,
                                         bias=bias[0:HALF, n:n + 1]).then_inc(evacuated, 1)
                nc.scalar.activation(direct_out, z[n][HALF:OUT, :], ACT.Relu,
                                     bias=bias[HALF:OUT, n:n + 1]).then_inc(evacuated, 1)

            def finish_last(c, exact_done):
                act.wait_ge(exact_used, exact_done)
                nc.scalar.activation(z[2][:, :], z[2][:, :], ACT.Relu, bias=bias[:, 2:3]).then_inc(z2_evacuated, 1)

            def round(i, d, first=False, more=True):
                c = 2 * i + d
                n1, n2 = KINDS[1].count(S), KINDS[2].count(S)
                split_hi(1, place(S, i, d, 1), range(0, 1), started=not first)
                if not first:
                    finish_last(c - 1, place(E, i, d, 1)[0])
                split_hi(1, place(S, i, d, 1), range(1, 4), started=not first)
                if more:
                    copy_fields(c + 1)
                split_hi(1, place(S, i, d, 1), range(4, n1), started=not first)
                if more:
                    split_hi(0, place(S, i, d, 0), range(KINDS[0].count(S)))
                act.wait_ge(exact_used, place(E, i, d, 0)[0])
                spread_maps(1, maps2, direct[HALF:OUT, :], z1_evacuated)
                split_hi(2, place(S, i, d, 2, more), range(0, 4))
                if more:
                    act.wait_ge(exact_used, place(E, i, d, 2)[0])
                    act.wait_ge(direct_summed, c + 1)
                    spread_maps(0, maps1, direct[0:HALF, :], z0_evacuated)
                split_hi(2, place(S, i, d, 2, more), range(4, n2))

            for part, (we, ws) in enumerate(((w_exact[0], w_staged[0]), (w0e_t, w0s_t))):
                act.dma_start(we[0:ROWS0, :, :], w0e[:, part, :, :]).then_inc(w0_loaded, 16)
                act.dma_start(ws[0:ROWS0, :, :], w0s[:, part, :, :]).then_inc(w0_loaded, 16)
            for n, b in enumerate((b0, b1, b2)):
                act.dma_start(bias[:, n:n + 1], b).then_inc(bias_loaded, 16)
            for n, we, ws in ((1, w1e, w1s), (2, w2e, w2s)):
                act.dma_start(w_staged[n], ws).then_inc(w_staged_loaded[n], 16)
                act.dma_start(w_exact[n][:, :, :], we).then_inc(w_exact_loaded[n], 16)
            act.wait_ge(w0_summed, 1)
            weights_split_hi(0)
            copy_fields(0)
            split_hi(0, (0, 0), range(KINDS[0].count(S)), started=False)
            act.wait_ge(w_staged_loaded[1], 16)
            weights_split_hi(1)
            act.wait_ge(w_staged_loaded[2], 16)
            weights_split_hi(2)
            act.wait_ge(bias_loaded, 48)
            act.wait_ge(exact_used, KINDS[0].count(E))
            spread_maps(0, maps1, direct[0:HALF, :], z0_evacuated)
            round(0, 0, first=True)
            with act.Fori(0, CHUNKS // 2 - 1) as i:
                round(i, 1)
                round(i, 2)
            round(CHUNKS // 2 - 1, 1, more=False)
            finish_last(CHUNKS - 1, PER_ROUND[E] * CHUNKS)


def kernel(r_inputs, L0_rec_w0, L0_rec_w1, L0_rec_w2, L0_rec_b0, L0_rec_b1, L0_rec_b2):
    import numpy as np
    import concourse.bacc as bacc
    from concourse import mybir as mb
    from concourse.bass_utils import run_bass_kernel_spmd

    x = np.asarray(r_inputs).reshape(CHUNKS, EXAMPLES, FIELDS, DIM).transpose(0, 2, 1, 3)
    x = x.reshape(CHUNKS, FIELDS, COLS)
    w0 = np.asarray(L0_rec_w0)
    pairs = np.zeros((GROUP, FIELDS, 2, TILES0, OUT), w0.dtype)
    i = np.arange(FIELDS)
    for shift in range(SHIFTS):
        t, g = divmod(shift, GROUP)
        j = (i + shift) % FIELDS
        pairs[g, :, 0, t] = w0[i, j]
        if shift:
            pairs[g, :, 1, t] = w0[j, i]
    pairs = pairs.reshape(ROWS0, 2, TILES0, OUT)
    arrays = {
        "x0": np.concatenate([x, x], axis=1),
        "w0e": pairs[:, :, tiles_of(0, E)],
        "w0s": pairs[:, :, tiles_of(0, S)],
    }
    for n, w in ((1, L0_rec_w1), (2, L0_rec_w2)):
        w = np.asarray(w).reshape(FIELDS * HALF, OUT)
        w = np.concatenate([w, np.zeros((TILES * 128 - len(w), OUT), w.dtype)])
        w = w.reshape(TILES, 128, OUT).transpose(1, 0, 2)
        arrays[f"w{n}e"] = w[:, tiles_of(n, E)]
        arrays[f"w{n}s"] = w[:, tiles_of(n, S)]
    for n, b in enumerate((L0_rec_b0, L0_rec_b1, L0_rec_b2)):
        arrays[f"b{n}"] = np.asarray(b).reshape(OUT, 1)
    nc = bacc.Bacc("TRN2", target_bir_lowering=False, num_devices=1)
    args = []
    for name, a in arrays.items():
        arrays[name] = np.ascontiguousarray(a)
        args.append(nc.dram_tensor(name, a.shape, mb.dt.from_np(a.dtype), kind="ExternalInput").ap())
    args.append(nc.dram_tensor("out", (2 * OUT, BATCH), mb.dt.float32, kind="ExternalOutput").ap())
    cin_kernel(nc, *args)
    r = run_bass_kernel_spmd(nc, [arrays], core_ids=[0])
    return np.ascontiguousarray(r.results[0]["out"].T)
```

```python
import concourse.bass as bass
from concourse import mybir
from contextlib import ExitStack

FIELDS = 39
DIM = 16
BATCH = 512
OUT = 128
HALF = OUT // 2
COLS = 512
EXAMPLES = COLS // DIM
CHUNKS = BATCH * DIM // COLS
SHIFTS = FIELDS // 2 + 1
GROUP = 3
ROWS0 = GROUP * FIELDS
TILES0 = -(-SHIFTS // GROUP)
LAST0 = (SHIFTS - GROUP * (TILES0 - 1)) * FIELDS
TILES = (FIELDS + 1) // 2

E, S, D = "E", "S", "D"
KINDS = ("EDEE", "SESSSESDES", "SESSESSDES")
COUPLES = tuple(len(k) for k in KINDS)
assert KINDS[0][-1] == E and KINDS[1][-1] == S and KINDS[2][-1] == S


def split_of(layer):
    return [k for k in range(COUPLES[layer]) if KINDS[layer][k] != E]


SPLIT_TILES = tuple(2 * len(split_of(n)) for n in range(3))
EXACT_TILES = (TILES0 - SPLIT_TILES[0], TILES - SPLIT_TILES[1], TILES - SPLIT_TILES[2])
LO_LAG = 2
D_LAG = 2
for _kinds in KINDS:
    assert all(D not in _kinds[k + 1:k + 1 + D_LAG] and k + D_LAG < len(_kinds)
               for k in range(len(_kinds)) if _kinds[k] == D)

EXACT_RING = 3
RAW_RING = 4
HI_RING = 5
LO_RING = 3

SUM_LAST_AT = 7
SUM_DIRECT_AT = 8
COPY_AT = 1
FINISH_AT = 3
MAPS1_AT = 6

WEIGHTS_LO = (1, 3, 5)
PARTS = COUPLES[1] // 2


def tiles_of(layer, kind):
    tiles = (TILES0, TILES, TILES)[layer]
    return [t for t in range(tiles) if (KINDS[layer][t // 2] == E) == (kind == E)]


def count_kind(kinds, kind):
    return sum(k in kind for k in kinds)


PER_ROUND = {kind: sum(count_kind(kinds, kind) for kinds in KINDS) for kind in (E, S, D, "SD")}
for _ring, _kind in ((EXACT_RING, E), (RAW_RING, S), (HI_RING, "SD"), (LO_RING, "SD")):
    assert 2 * PER_ROUND[_kind] % _ring == 0


def place(kind, i, d, layer, k=0, more=True):
    at = {1: 0, 0: count_kind(KINDS[1], kind), 2: count_kind(KINDS[1], kind) + more * count_kind(KINDS[0], kind)}
    first = count_kind(KINDS[0], kind) + PER_ROUND[kind] * d + at[layer] + count_kind(KINDS[layer][:k], kind)
    if d < 0:
        first = count_kind(KINDS[0][:k], kind)
    return first + 2 * PER_ROUND[kind] * i, first


def cin_kernel(nc, x0, w0e, w0s, w1e, w1s, w2e, w2s, b, out):
    fp32 = mybir.dt.float32
    fp32r = mybir.dt.float32r
    ALU = mybir.AluOpType
    ACT = mybir.ActivationFunctionType
    AX = mybir.AxisListType

    ctx = ExitStack()
    with ctx:
        def sb(name, shape, dt=fp32):
            return ctx.enter_context(nc.sbuf_tensor(name, shape, dt))

        def pb(name, shape):
            return ctx.enter_context(nc.psum_tensor(name, shape, fp32))

        def sem(name):
            return ctx.enter_context(nc.semaphore(name))

        w_exact = [sb(f"w{n}_exact", [128, EXACT_TILES[n], OUT]) for n in range(3)]
        w_hi = [sb(f"w{n}_hi", [128, SPLIT_TILES[n], OUT], fp32r) for n in range(3)]
        w_lo = [sb(f"w{n}_lo", [128, SPLIT_TILES[n], OUT], fp32r) for n in range(3)]
        bias = sb("bias", [128, 3])
        field_copies = sb("field_copies", [128, COLS])
        field_shifts = sb("field_shifts", [128, TILES0, COLS])
        field_spread = sb("field_spread", [128, 2, TILES, COLS])
        exact = sb("exact", [128, EXACT_RING, 2, COLS])
        raw = sb("raw", [128, RAW_RING, 2, COLS])
        hi = sb("hi", [128, HI_RING, 2, COLS], fp32r)
        lo = sb("lo", [128, LO_RING, 2, COLS], fp32r)
        direct = sb("direct", [128, COLS])
        sums = sb("sums", [128, 2, BATCH])

        staging = field_spread[:, 1, :, :].rearrange("p t c -> p (t c)")
        staged_tiles = 0

        def stage(tiles):
            nonlocal staged_tiles
            staged_tiles += tiles
            return staging[:, (staged_tiles - tiles) * OUT:staged_tiles * OUT].rearrange("p (t s) -> p t s", s=OUT)

        w_staged = [stage(SPLIT_TILES[n]) for n in range(3)]
        w0s_parts = stage(2 * SPLIT_TILES[0])
        w0e_parts = stage(2 * EXACT_TILES[0])

        z = [pb(f"z{n}", [128, COLS]) for n in range(3)]
        maps1 = pb("maps1", [128, COLS])
        maps2 = pb("maps2", [128, COLS])
        copies = pb("copies", [128, COLS])
        d_raw = pb("d_raw", [128, 2, COLS])

        w0s_loaded = sem("w0s_loaded")
        w0e_loaded = sem("w0e_loaded")
        w_staged_loaded = [None, sem("w1_staged_loaded"), sem("w2_staged_loaded")]
        w_exact_loaded = [None, sem("w1_exact_loaded"), sem("w2_exact_loaded")]
        w0s_summed = sem("w0s_summed")
        w0e_summed = sem("w0e_summed")
        weights_hi = sem("weights_hi")
        weights_lo = sem("weights_lo")
        bias_loaded = sem("bias_loaded")
        copies_loaded = sem("copies_loaded")
        shifts_loaded = [sem("shifts_loaded0"), sem("shifts_loaded1")]
        spread_loaded = [[sem(f"spread_loaded{p}{q}") for q in range(PARTS)] for p in range(2)]
        copies_ready = sem("copies_ready")
        exact_ready = sem("exact_ready")
        exact_used = sem("exact_used")
        raw_ready = sem("raw_ready")
        s_lo_ready = sem("s_lo_ready")
        d_raw_ready = sem("d_raw_ready")
        d_lo_ready = sem("d_lo_ready")
        hi_ready = sem("hi_ready")
        lo_used = sem("lo_used")
        z0_evacuated = sem("z0_evacuated")
        z1_evacuated = sem("z1_evacuated")
        z2_evacuated = sem("z2_evacuated")
        direct_summed = sem("direct_summed")
        last_summed = sem("last_summed")
        stored = sem("stored")

        def loads(i, d):
            return i + d // 2 + 1

        block = ctx.enter_context(nc.Block())

        @block.sync
        def _(sp):
            def load_copies(c):
                for g in range(GROUP):
                    sp.dma_start(field_copies[g * FIELDS:(g + 1) * FIELDS, :],
                                 x0[c, 0:FIELDS, :]).then_inc(copies_loaded, 16)

            def load_shifts(c, part):
                for g in range(GROUP):
                    start, end = ((0, 2), (2, TILES0))[part]
                    if g * FIELDS >= LAST0 and end == TILES0:
                        end -= 1
                    base = x0[c, GROUP * start + g:GROUP * start + g + FIELDS, :]
                    src = bass.AP(tensor=base.tensor, offset=base.offset,
                                  ap=[[COLS, FIELDS], [GROUP * COLS, end - start], [1, COLS]])
                    sp.dma_start(field_shifts[g * FIELDS:(g + 1) * FIELDS, start:end, :],
                                 src).then_inc(shifts_loaded[part], 16)

            def load_fields(c):
                load_copies(c)
                load_shifts(c, 0)
                load_shifts(c, 1)

            def load_spread(c, par, q):
                for half in range(2):
                    row = FIELDS + 8 * q + half
                    base = x0[c, row:row + 1, :]
                    src = bass.AP(tensor=base.tensor, offset=base.offset,
                                  ap=[[0, HALF], [2 * COLS, 4], [1, COLS]])
                    sp.dma_start(field_spread[half * HALF:(half + 1) * HALF, par, 4 * q:4 * q + 4, :],
                                 src).then_inc(spread_loaded[par][q], 16)

            def wait_multiplied(i, d, layer, couples):
                kind = KINDS[layer][couples - 1]
                sp.wait_ge({E: exact_ready, S: raw_ready, D: d_raw_ready}[kind], place(kind, i, d, layer, couples)[0])

            def load_weights(n, exact_part, split_part):
                sp.dma_start(w_staged[n], split_part).then_inc(w_staged_loaded[n], 16)
                sp.dma_start(w_exact[n][:, :, :], exact_part).then_inc(w_exact_loaded[n], 16)

            load_fields(0)
            load_weights(1, w1e, w1s)
            for q in range(PARTS):
                load_spread(0, 0, q)
            sp.wait_ge(exact_ready, KINDS[0].count(E))
            load_fields(1)
            load_weights(2, w2e, w2s)
            sp.wait_ge(weights_lo, WEIGHTS_LO[2])
            for q in range(PARTS):
                load_spread(1, 1, q)

            def refill(i, d):
                c = 2 * i + d
                wait_multiplied(i, d, 0, COUPLES[0])
                load_fields(c + 2)
                for q in range(PARTS):
                    wait_multiplied(i, d, 2, 2 * q + 2)
                    load_spread(c + 2, d % 2, q)

            with sp.Fori(0, CHUNKS // 2 - 1) as i:
                refill(i, 0)
                refill(i, 1)

            sp.wait_ge(direct_summed, CHUNKS)
            sp.dma_start(out[0:OUT, :], sums[:, 0, :]).then_inc(stored, 16)
            sp.wait_ge(last_summed, CHUNKS)
            sp.dma_start(out[OUT:2 * OUT, :], sums[:, 1, :]).then_inc(stored, 16)
            sp.wait_ge(stored, 32)

        @block.vector
        def _(dve):
            def multiply(layer, by, spread, rows_of, i, d, couples, more, wait_loaded):
                for k in couples:
                    kind = KINDS[layer][k]
                    count, slot = place(kind, i, d, layer, k, more)
                    tiles = min(2, (TILES0, TILES, TILES)[layer] - 2 * k)
                    rows = rows_of(k)
                    wait_loaded(k)
                    if kind == E:
                        if slot >= EXACT_RING:
                            dve.wait_ge(exact_used, count - EXACT_RING + 1)
                        ring, ready = exact[0:rows, slot % EXACT_RING, 0:tiles, :], exact_ready
                    elif kind == S:
                        if slot >= RAW_RING:
                            dve.wait_ge(s_lo_ready, count - RAW_RING + 1)
                        ring, ready = raw[0:rows, slot % RAW_RING, 0:tiles, :], raw_ready
                    else:
                        if slot >= 1:
                            dve.wait_ge(d_lo_ready, count)
                        ring, ready = d_raw[0:rows, 0:tiles, :], d_raw_ready
                    nc.vector.tensor_tensor(ring, spread[0:rows, 2 * k:2 * k + tiles, :],
                                            by[0:rows, :].unsqueeze(1).to_broadcast([rows, tiles, COLS]),
                                            ALU.mult).then_inc(ready, 1)
                    if k >= D_LAG and KINDS[layer][k - D_LAG] == D:
                        split_lo_couple(layer, place("SD", i, d, layer, k - D_LAG, more))

            def split_lo_couple(layer, counts):
                count, slot = counts
                rows = 128 if layer else ROWS0
                dve.wait_ge(hi_ready, count + 1)
                if slot >= LO_RING:
                    dve.wait_ge(lo_used, count - LO_RING + 1)
                nc.vector.tensor_tensor(lo[0:rows, slot % LO_RING, :, :], d_raw[0:rows, :, :],
                                        hi[0:rows, slot % HI_RING, :, :].bitcast(fp32),
                                        ALU.subtract).then_inc(d_lo_ready, 1)

            def multiply0(i, d, couples=range(COUPLES[0])):
                c = 2 * i + d
                dve.wait_ge(copies_ready, c + 2)

                def wait_loaded(k):
                    if k < 2:
                        dve.wait_ge(shifts_loaded[k], (c + 2) * GROUP * 16)

                multiply(0, copies, field_shifts, lambda k: ROWS0 if k < COUPLES[0] - 1 else LAST0,
                         i, d, couples, True, wait_loaded)

            def multiply12(layer, i, d, couples, more=True):
                def wait_loaded(k):
                    if layer == 1 and k % 2 == 0:
                        dve.wait_ge(spread_loaded[d % 2][k // 2], loads(i, d) * 32)

                multiply(layer, maps1 if layer == 1 else maps2, field_spread[:, d % 2, :, :],
                         lambda k: 128, i, d, couples, more, wait_loaded)

            def sum_direct(c):
                dve.wait_ge(z0_evacuated, 3 * c + 3)
                dve.wait_ge(z1_evacuated, 3 * c + 3)
                nc.vector.tensor_reduce(sums[:, 0, bass.ds(c * EXAMPLES, EXAMPLES)],
                                        direct[:, :].rearrange("p (b d) -> p b d", d=DIM),
                                        AX.X, ALU.add).then_inc(direct_summed, 1)

            def sum_last(c):
                dve.wait_ge(z2_evacuated, c + 1)
                nc.vector.tensor_reduce(sums[:, 1, bass.ds(c * EXAMPLES, EXAMPLES)],
                                        z[2][:, :].rearrange("p (b d) -> p b d", d=DIM),
                                        AX.X, ALU.add).then_inc(last_summed, 1)

            def split_lo(n):
                rows, tiles = (ROWS0, SPLIT_TILES[0]) if n == 0 else (128, SPLIT_TILES[n] - 1)
                dve.wait_ge(weights_hi, n + 1)
                nc.vector.tensor_tensor(w_lo[n][0:rows, 0:tiles, :], w_staged[n][0:rows, 0:tiles, :],
                                        w_hi[n][0:rows, 0:tiles, :].bitcast(fp32),
                                        ALU.subtract).then_inc(weights_lo, 1)
                if n > 0:
                    nc.vector.tensor_tensor(w_hi[n][HALF:128, tiles, :], w_staged[n][HALF:128, tiles, :],
                                            w_hi[n][HALF:128, tiles, :].bitcast(fp32),
                                            ALU.subtract).then_inc(weights_lo, 1)

            def round(i, d, first=False, more=True):
                c = 2 * i + d
                dve.wait_ge(z0_evacuated, 3 * c + 2)
                multiply12(1, i, d, range(0, SUM_LAST_AT))
                if not first:
                    sum_last(c - 1)
                multiply12(1, i, d, range(SUM_LAST_AT, COUPLES[1]))
                if more:
                    multiply0(i, d)
                if first:
                    split_lo(2)
                dve.wait_ge(z1_evacuated, 3 * c + 2)
                multiply12(2, i, d, range(0, SUM_DIRECT_AT), more)
                sum_direct(c)
                multiply12(2, i, d, range(SUM_DIRECT_AT, COUPLES[2]), more)

            def sum_weights0(out_tiles, parts, tiles, loaded, summed):
                dve.wait_ge(loaded, 16)
                nc.vector.tensor_tensor(out_tiles[0:ROWS0, :, :], parts[0:ROWS0, 0:tiles, :],
                                        parts[0:ROWS0, tiles:2 * tiles, :], ALU.add).then_inc(summed, 1)

            sum_weights0(w_exact[0], w0e_parts, EXACT_TILES[0], w0e_loaded, w0e_summed)
            multiply0(0, -1, range(0, 1))
            sum_weights0(w_staged[0], w0s_parts, SPLIT_TILES[0], w0s_loaded, w0s_summed)
            multiply0(0, -1, range(1, 2))
            split_lo(0)
            multiply0(0, -1, range(2, COUPLES[0]))
            split_lo(1)
            round(0, 0, first=True)
            with dve.Fori(0, CHUNKS // 2 - 1) as i:
                round(i, 1)
                round(i, 2)
            round(CHUNKS // 2 - 1, 1, more=False)
            sum_last(CHUNKS - 1)

        @block.gpsimd
        def _(pool):
            def split_lo(layer, i, d, more=True):
                rows = ROWS0 if layer == 0 else 128
                for k in range(COUPLES[layer]):
                    if KINDS[layer][k] == S:
                        count, slot = place("SD", i, d, layer, k, more)
                        raw_slot = place(S, i, d, layer, k, more)[1]
                        pool.wait_ge(hi_ready, count + 1)
                        if slot >= LO_RING:
                            pool.wait_ge(lo_used, count - LO_RING + 1)
                        nc.gpsimd.tensor_tensor(lo[0:rows, slot % LO_RING, :, :],
                                                raw[0:rows, raw_slot % RAW_RING, :, :],
                                                hi[0:rows, slot % HI_RING, :, :].bitcast(fp32),
                                                ALU.subtract).then_inc(s_lo_ready, 1)

            def round(i, d, more=True):
                split_lo(1, i, d)
                if more:
                    split_lo(0, i, d)
                split_lo(2, i, d, more)

            split_lo(0, 0, -1)
            round(0, 0)
            with pool.Fori(0, CHUNKS // 2 - 1) as i:
                round(i, 1)
                round(i, 2)
            round(CHUNKS // 2 - 1, 1, more=False)

        @block.tensor
        def _(pe):
            def schedule(layer):
                todo, pending = [], []
                for k, kind in enumerate(KINDS[layer]):
                    todo.append(("exact" if kind == E else "hi", k))
                    if kind != E:
                        pending.append(k)
                    if pending and k - pending[0] >= LO_LAG and pending[0] != split_of(layer)[-1]:
                        todo.append(("lo", pending.pop(0)))
                return todo + [("lo", k) for k in pending]

            def contract(layer, i, d, more=True):
                tiles = (TILES0, TILES, TILES)[layer]
                order = schedule(layer)
                for step, (what, k) in enumerate(order):
                    kind = KINDS[layer][k]
                    count, slot = place(E if kind == E else "SD", i, d, layer, k, more)
                    m = count_kind(KINDS[layer][:k], E if kind == E else "SD")
                    if what == "exact":
                        pe.wait_ge(exact_ready, count + 1)
                        if d < 0 and m == 0:
                            pe.wait_ge(w0e_summed, 1)
                    elif what == "hi":
                        pe.wait_ge(hi_ready, count + 1)
                        if d < 0 and m == 0:
                            pe.wait_ge(weights_lo, WEIGHTS_LO[0])
                    else:
                        pe.wait_ge(s_lo_ready if kind == S else d_lo_ready, place(kind, i, d, layer, k, more)[0] + 1)
                    e, h, l = (slot % ring for ring in (EXACT_RING, HI_RING, LO_RING))
                    passes = []
                    for j in range(min(2, tiles - 2 * k)):
                        t = 2 * m + j
                        last = 2 * k + j == tiles - 1
                        rows = 128 if layer else LAST0 if last else ROWS0
                        if what == "exact":
                            passes += [(w_exact[layer][:, t, :], exact[:, e, j, :], rows)]
                        elif what == "hi":
                            passes += [(w_hi[layer][:, t, :], hi[:, h, j, :], rows)]
                            if not (layer and last):
                                passes += [(w_lo[layer][:, t, :], hi[:, h, j, :], rows)]
                        else:
                            passes += [(w_hi[layer][:, t, :], lo[:, l, j, :], rows)]
                    for p, (w, part, rows) in enumerate(passes):
                        mm = nc.tensor.matmul(z[layer][:, :], w[0:rows, :], part[0:rows, :],
                                              start=(step == 0 and p == 0),
                                              stop=(step == len(order) - 1 and p == len(passes) - 1))
                    if what != "hi":
                        mm.then_inc(exact_used if what == "exact" else lo_used, 1)

            def round(i, d, first=False, more=True):
                c = 2 * i + d
                if not first:
                    pe.wait_ge(z1_evacuated, 3 * c)
                contract(1, i, d)
                if more:
                    pe.wait_ge(z0_evacuated, 3 * c + 3)
                    contract(0, i, d)
                if first:
                    pe.wait_ge(w_exact_loaded[2], 16)
                    pe.wait_ge(weights_lo, WEIGHTS_LO[2])
                else:
                    pe.wait_ge(last_summed, c)
                contract(2, i, d, more)

            contract(0, 0, -1)
            pe.wait_ge(w_exact_loaded[1], 16)
            pe.wait_ge(weights_lo, WEIGHTS_LO[1])
            round(0, 0, first=True)
            with pe.Fori(0, CHUNKS // 2 - 1) as i:
                round(i, 1)
                round(i, 2)
            round(CHUNKS // 2 - 1, 1, more=False)

        @block.scalar
        def _(act):
            def split_hi(layer, i, d, couples, more=True):
                rows = ROWS0 if layer == 0 else 128
                for k in couples:
                    kind = KINDS[layer][k]
                    count, slot = place("SD", i, d, layer, k, more)
                    kind_count, kind_slot = place(kind, i, d, layer, k, more)
                    act.wait_ge(raw_ready if kind == S else d_raw_ready, kind_count + 1)
                    if slot >= HI_RING:
                        act.wait_ge(lo_used, count - HI_RING + 1)
                    products = raw[0:rows, kind_slot % RAW_RING, :, :] if kind == S else d_raw[0:rows, :, :]
                    nc.scalar.activation(hi[0:rows, slot % HI_RING, :, :], products,
                                         ACT.Copy).then_inc(hi_ready, 1)

            def weights_split_hi(n):
                rows = ROWS0 if n == 0 else 128
                nc.scalar.activation(w_hi[n][0:rows, :, :], w_staged[n][0:rows, :, :],
                                     ACT.Copy).then_inc(weights_hi, 1)

            def copy_fields(c):
                act.wait_ge(copies_loaded, (c + 1) * GROUP * 16)
                nc.scalar.activation(copies[0:ROWS0, :], field_copies[0:ROWS0, :], ACT.Copy).then_inc(copies_ready, 1)

            def spread_maps(n, maps, direct_out, evacuated):
                for half in range(2):
                    nc.scalar.activation(maps[half * HALF:(half + 1) * HALF, :], z[n][0:HALF, :], ACT.Relu,
                                         bias=bias[0:HALF, n:n + 1]).then_inc(evacuated, 1)
                nc.scalar.activation(direct_out, z[n][HALF:OUT, :], ACT.Relu,
                                     bias=bias[HALF:OUT, n:n + 1]).then_inc(evacuated, 1)

            def finish_last(c, used):
                act.wait_ge(lo_used, used)
                nc.scalar.activation(z[2][:, :], z[2][:, :], ACT.Relu, bias=bias[:, 2:3]).then_inc(z2_evacuated, 1)

            def round(i, d, first=False, more=True):
                c = 2 * i + d
                for m, k in enumerate(split_of(1)):
                    if m == COPY_AT and more and not first:
                        copy_fields(c + 1)
                    if m == FINISH_AT and not first:
                        finish_last(c - 1, place("SD", i, d, 1)[0])
                    split_hi(1, i, d, [k])
                if first:
                    copy_fields(1)
                    act.wait_ge(w_staged_loaded[2], 16)
                    weights_split_hi(2)
                if more:
                    split_hi(0, i, d, split_of(0))
                act.wait_ge(lo_used, place("SD", i, d, 0)[0])
                spread_maps(1, maps2, direct[HALF:OUT, :], z1_evacuated)
                for m, k in enumerate(split_of(2)):
                    if m == MAPS1_AT and more:
                        act.wait_ge(lo_used, place("SD", i, d, 2)[0])
                        act.wait_ge(direct_summed, c + 1)
                        spread_maps(0, maps1, direct[0:HALF, :], z0_evacuated)
                    split_hi(2, i, d, [k], more)

            act.dma_start(w0e_parts[0:ROWS0, :, :], w0e).then_inc(w0e_loaded, 16)
            act.dma_start(w0s_parts[0:ROWS0, :, :], w0s).then_inc(w0s_loaded, 16)
            act.dma_start(bias[:, :], b).then_inc(bias_loaded, 16)
            copy_fields(0)
            act.wait_ge(w0s_summed, 1)
            weights_split_hi(0)
            split_hi(0, 0, -1, split_of(0))
            act.wait_ge(w_staged_loaded[1], 16)
            weights_split_hi(1)
            act.wait_ge(bias_loaded, 16)
            act.wait_ge(lo_used, len(split_of(0)))
            spread_maps(0, maps1, direct[0:HALF, :], z0_evacuated)
            round(0, 0, first=True)
            with act.Fori(0, CHUNKS // 2 - 1) as i:
                round(i, 1)
                round(i, 2)
            round(CHUNKS // 2 - 1, 1, more=False)
            finish_last(CHUNKS - 1, PER_ROUND["SD"] * CHUNKS)


def kernel(r_inputs, L0_rec_w0, L0_rec_w1, L0_rec_w2, L0_rec_b0, L0_rec_b1, L0_rec_b2):
    import numpy as np
    import concourse.bacc as bacc
    from concourse import mybir as mb
    from concourse.bass_utils import run_bass_kernel_spmd

    x = np.asarray(r_inputs).reshape(CHUNKS, EXAMPLES, FIELDS, DIM).transpose(0, 2, 1, 3)
    x = x.reshape(CHUNKS, FIELDS, COLS)
    w0 = np.asarray(L0_rec_w0)
    pairs = np.zeros((GROUP, FIELDS, 2, TILES0, OUT), w0.dtype)
    i = np.arange(FIELDS)
    for shift in range(SHIFTS):
        t, g = divmod(shift, GROUP)
        j = (i + shift) % FIELDS
        pairs[g, :, 0, t] = w0[i, j]
        if shift:
            pairs[g, :, 1, t] = w0[j, i]
    pairs = pairs.reshape(ROWS0, 2, TILES0, OUT)
    arrays = {
        "x0": np.concatenate([x, x, x[:, -1:]], axis=1),
        "w0e": pairs[:, :, tiles_of(0, E)].reshape(ROWS0, -1, OUT),
        "w0s": pairs[:, :, tiles_of(0, S)].reshape(ROWS0, -1, OUT),
    }
    for n, w in ((1, L0_rec_w1), (2, L0_rec_w2)):
        w = np.asarray(w).reshape(FIELDS * HALF, OUT)
        w = np.concatenate([w, w[-HALF:]])
        w = w.reshape(TILES, 128, OUT).transpose(1, 0, 2)
        arrays[f"w{n}e"] = w[:, tiles_of(n, E)]
        arrays[f"w{n}s"] = w[:, tiles_of(n, S)]
    arrays["b"] = np.stack([np.asarray(b) for b in (L0_rec_b0, L0_rec_b1, L0_rec_b2)], axis=1)
    nc = bacc.Bacc("TRN2", target_bir_lowering=False, num_devices=1)
    args = []
    for name, a in arrays.items():
        arrays[name] = np.ascontiguousarray(a)
        args.append(nc.dram_tensor(name, a.shape, mb.dt.from_np(a.dtype), kind="ExternalInput").ap())
    args.append(nc.dram_tensor("out", (2 * OUT, BATCH), mb.dt.float32, kind="ExternalOutput").ap())
    cin_kernel(nc, *args)
    r = run_bass_kernel_spmd(nc, [arrays], core_ids=[0])
    return np.ascontiguousarray(r.results[0]["out"].T)
```
